# Optimizing a Trainium2 kernel written in Bass

```python
import numpy as np
import jax
import jax.numpy as jnp

def _softmax(x, axis=-1):
    return jax.nn.softmax(x, axis=axis)

def _gelu(x):
    return jax.nn.gelu(x, approximate=True)

def _silu(x):
    return jax.nn.silu(x)

def _sigmoid(x):
    return jax.nn.sigmoid(x)

def _layernorm(x, axis=-1, eps=1e-05):
    m = jnp.mean(x, axis=axis, keepdims=True)
    v = jnp.var(x, axis=axis, keepdims=True)
    return (x - m) / jnp.sqrt(v + eps)

def _scatter_add(tgt, idx, src, axis=0):
    return tgt.at[idx].add(src)

def _segment_sum(src, seg, n):
    return jax.ops.segment_sum(src, seg, n)
kernel_name = 'mk_adaln_ffn_d1_seqx_r4_6b18a5'

def setup_inputs(seed: int=0):
    np.random.seed(seed)
    _w = jnp.asarray

    def _rec_inputs():
        import jax
        import jax.numpy as jnp
        _rk = jax.random.key(seed)
        x = -0.000125 + 0.9999 * jax.random.normal(jax.random.fold_in(_rk, 1), (8, 256, 1024), jnp.float32)
        _lenS = 256 - jax.random.randint(jax.random.fold_in(_rk, 7), (8,), 0, max(1, 256 // 4) + 1, jnp.int32)
        _lenS2 = 256 - jax.random.randint(jax.random.fold_in(_rk, 8), (8,), 0, max(1, 256 // 4) + 1, jnp.int32)
        itok_B_3_7 = jax.random.randint(jax.random.fold_in(_rk, 11), (8,), 3, 8, jnp.int32)
        return (x, itok_B_3_7)
    x, itok_B_3_7 = _rec_inputs()

    def _L0_cond_setup():
        import jax, jax.numpy as jnp
        import numpy as np
        MAX_LORAS, OUT, IN = (8, 1024, 1024)
        B, S = (4, 512)
        key = jax.random.key(seed)
        k1, k2, k3 = jax.random.split(key, 3)
        x = jax.random.normal(k1, (B, S, IN), dtype=jnp.float32)
        weight = jax.random.normal(k2, (MAX_LORAS, OUT, IN), dtype=jnp.float32) * 0.02
        adapter_ids = jax.random.randint(k3, (B,), 0, MAX_LORAS, dtype=jnp.int32)
        return {'x': x, 'weight': weight, 'adapter_ids': adapter_ids}
    _L0_cond_all = _L0_cond_setup()
    _L0_cond_in = {k: v for k, v in _L0_cond_all.items() if k in ('weight',)}
    del _L0_cond_all

    def _L0_ffn_setup():
        import jax, jax.numpy as jnp
        import numpy as np
        NUM_EXPERTS = 4
        HIDDEN = 1024
        RANK = 8
        ALPHA = 8.0
        SCALE = ALPHA / RANK
        key = jax.random.key(seed)
        ks = jax.random.split(key, 6)
        B, T, H, E, R = (4, 1024, HIDDEN, NUM_EXPERTS, RANK)
        x = jax.random.normal(ks[0], (B, T, H), dtype=jnp.float32)
        W_up = jax.random.normal(ks[1], (H, H), dtype=jnp.float32) / np.sqrt(H)
        gate_w = jax.random.normal(ks[2], (E, H), dtype=jnp.float32) / np.sqrt(H)
        expert_bias = jnp.zeros((E,), dtype=jnp.float32)
        lora_A = jax.random.normal(ks[3], (E, R, H), dtype=jnp.float32) / np.sqrt(H)
        lora_B = jax.random.normal(ks[4], (E, H, R), dtype=jnp.float32) * 0.01
        return {'x': x, 'W_up': W_up, 'gate_w': gate_w, 'expert_bias': expert_bias, 'lora_A': lora_A, 'lora_B': lora_B}
    _L0_ffn_all = _L0_ffn_setup()
    _L0_ffn_in = {k: v for k, v in _L0_ffn_all.items() if k in ('W_up', 'gate_w', 'expert_bias', 'lora_A', 'lora_B')}
    del _L0_ffn_all
    return {'x': x, 'itok_B_3_7': itok_B_3_7, 'L0_cond_weight': _L0_cond_in['weight'], 'L0_ffn_W_up': _L0_ffn_in['W_up'], 'L0_ffn_gate_w': _L0_ffn_in['gate_w'], 'L0_ffn_expert_bias': _L0_ffn_in['expert_bias'], 'L0_ffn_lora_A': _L0_ffn_in['lora_A'], 'L0_ffn_lora_B': _L0_ffn_in['lora_B']}

def reference(x, itok_B_3_7, L0_cond_weight, L0_ffn_W_up, L0_ffn_gate_w, L0_ffn_expert_bias, L0_ffn_lora_A, L0_ffn_lora_B):
    import jax
    import jax.numpy as jnp

    def _L0_cond_ref(x, weight, adapter_ids):
        import jax, jax.numpy as jnp
        import numpy as np
        MAX_LORAS, OUT, IN = (8, 1024, 1024)
        B, S = (4, 512)
        w = weight[adapter_ids]
        return jnp.einsum('bsi,boi->bso', x, w)

    def _L0_ffn_ref(x, W_up, gate_w, expert_bias, lora_A, lora_B):
        import jax, jax.numpy as jnp
        import numpy as np
        NUM_EXPERTS = 4
        HIDDEN = 1024
        RANK = 8
        ALPHA = 8.0
        SCALE = ALPHA / RANK
        B, T, H = x.shape
        E = gate_w.shape[0]
        x_flat = x.reshape(-1, H)
        logits = x_flat @ gate_w.T + expert_bias
        top1 = jnp.argmax(logits, axis=-1)
        one_hot = jax.nn.one_hot(top1, E, dtype=x_flat.dtype)
        base_out = jnp.einsum('bth,oh->bto', x, W_up)
        z = jnp.einsum('nh,erh->ner', x_flat, lora_A)
        d = jnp.einsum('ner,ehr->neh', z, lora_B) * SCALE
        delta = jnp.einsum('neh,ne->nh', d, one_hot)
        return base_out + delta.reshape(B, T, H)
    x = x + _L0_ffn_ref(_L0_cond_ref(x, L0_cond_weight, itok_B_3_7), L0_ffn_W_up, L0_ffn_gate_w, L0_ffn_expert_bias, L0_ffn_lora_A, L0_ffn_lora_B)
    return x

_drawn_inputs = setup_inputs


def setup_inputs(seed=0):
    import zlib

    import numpy as np

    out = dict(_drawn_inputs(seed))
    spreads = {'L0_ffn_expert_bias': (0.0, 0.8)}
    factors = {'L0_ffn_gate_w': 4.311, 'L0_ffn_lora_A': 3.694, 'L0_ffn_lora_B': 3.695}
    for name, (base, spread) in spreads.items():
        noise = np.random.default_rng([zlib.crc32(name.encode()), seed]).standard_normal(out[name].shape)
        drawn = base * np.exp(spread * noise) if base else spread * noise
        out[name] = jnp.asarray(drawn.astype(out[name].dtype))
    for name, factor in factors.items():
        out[name] = (out[name] * factor).astype(out[name].dtype)
    return out
```

```python
from contextlib import ExitStack

import concourse.bass as bass
from concourse import mybir

P = 128
F32 = mybir.dt.float32
F32R = mybir.dt.float32r
I32 = mybir.dt.int32
ALU = mybir.AluOpType
AX_X = mybir.AxisListType.X


def build(nc, xT, x, ids, w, w_up, gl, lora_b, bias, out):
    B, S, H = x.shape
    A = w.shape[0]
    KC = H // P
    OC = H // P
    T = S // P
    E = bias.shape[1]
    ER = lora_b.shape[0]
    R = ER // E
    GL = ER + E
    NW = H + 2 * GL
    RING = 4
    XH = 2
    XK = KC // XH
    CUT = (NW // 3 + 1) // 2 * 2
    BANK_C = H - 2 * CUT
    STEPS = 8
    assert T == 2 and 4 * ER == P and BANK_C + 2 * GL <= 512 and B >= 3

    with ExitStack() as ctx:
        def sb(name, shape, dt=F32):
            return ctx.enter_context(nc.sbuf_tensor(name, shape, dt))

        def sem(name):
            return ctx.enter_context(nc.semaphore(name))

        w_raw = sb("w_raw", [P, RING, KC * P])
        w_hi = sb("w_hi", [P, RING, KC * P], F32R)
        w_lo = sb("w_lo", [P, RING, KC * P], F32R)
        x_raw = sb("x_raw", [P, KC, S])
        x_hilo = sb("x_hilo", [P, KC, 2 * S], F32R)
        up_raw = sb("up_raw", [P, RING, H])
        up_hi = sb("up_hi", [P, OC, NW], F32R)
        up_lo = sb("up_lo", [P, OC, H], F32R)
        gl_raw = sb("gl_raw", [P, OC, GL])
        y_small = sb("y_small", [P, 2, S])
        y_full = sb("y_full", [P, 2, S])
        y_hi = sb("y_hi", [P, OC, S], F32R)
        y_lo = sb("y_lo", [P, OC, S], F32R)
        rows = sb("rows", [P, T, H])
        lb_raw = sb("lb_raw", [P, H])
        lb_parts = sb("lb_parts", [P, H], F32R)
        bias_sb = sb("bias_sb", [P, E])
        rank = sb("rank", [P, E])
        eye_f = sb("eye_f", [P, P])
        eye = sb("eye", [P, P], F32R)
        zlo = sb("zlo", [P, T, GL])
        zg = sb("zg", [P, T, GL])
        lg = sb("lg", [P, T, E])
        lmax = sb("lmax", [P, T])
        score = sb("score", [P, T, E])
        smax = sb("smax", [P, T])
        zm = sb("zm", [P, T, ER])
        z_parts = sb("z_parts", [P, T, P], F32R)
        zT = sb("zT", [P, T, P], F32R)

        ps_y = [ctx.enter_context(nc.psum_tensor(f"ps_y{i}", [P, 512], F32)) for i in range(2)]
        ps_o = [ctx.enter_context(nc.psum_tensor(f"ps_o{t}", [P, 3, 512], F32)) for t in range(T)]

        x_raw_in = [sem(f"x_raw_in{h}") for h in range(XH)]
        w_raw_in = [sem(f"w_raw_in{s}") for s in range(RING)]
        up_raw_in = [sem(f"up_raw_in{s}") for s in range(RING)]
        rows_in = [sem(f"rows_in{t}") for t in range(T)]
        gl_in = sem("gl_in")
        lb_in = sem("lb_in")
        bias_in = sem("bias_in")
        x_hi_ready = sem("x_hi_ready")
        x_ready = sem("x_ready")
        w_hi_ready = sem("w_hi_ready")
        w_ready = sem("w_ready")
        up_hi_ready = sem("up_hi_ready")
        up_ready = sem("up_ready")
        gl_hi_ready = sem("gl_hi_ready")
        gl_ready = sem("gl_ready")
        lb_hi_ready = sem("lb_hi_ready")
        lb_ready = sem("lb_ready")
        eye_step = sem("eye_step")
        eye_ready = sem("eye_ready")
        rank_ready = sem("rank_ready")
        y_done = sem("y_done")
        y_small_ready = sem("y_small_ready")
        y_full_ready = sem("y_full_ready")
        y_hi_ready = sem("y_hi_ready")
        y_ready = sem("y_ready")
        z_done = sem("z_done")
        z_step = sem("z_step")
        z_parts_ready = sem("z_parts_ready")
        zt_done = sem("zt_done")
        zt_ready = sem("zt_ready")
        out_done = sem("out_done")
        out_ready = sem("out_ready")
        stored = [sem(f"stored{t}") for t in range(T)]

        block = ctx.enter_context(nc.Block())

        @block.sync
        def _(sp):
            def adapter(b):
                i = sp.value_load(ids[0:1, b:b + 1] if isinstance(b, int) else ids[0:1, bass.ds(b, 1)])
                i = i + (i < 0) * A
                i = i * (i > -1)
                i = i + (i > A - 1) * (A - 1 - i)
                return sp.snap(i, min_val=0, max_val=A - 1)

            def load_w(b, c, i):
                if not (isinstance(b, int) and b == 0 and c < RING):
                    sp.wait_ge(w_ready, b * OC + c - RING + 1)
                sp.dma_start(w_raw[:, c % RING, :], w[bass.ds(i * OC + c, 1), :, :].rearrange("a p n -> (a p) n")
                             ).then_inc(w_raw_in[c % RING], 16)

            def load_x(b, h):
                if not (isinstance(b, int) and b == 0):
                    sp.wait_ge(x_ready, (b - 1) * XH + h + 1)
                sp.dma_start(x_raw[:, h * XK:(h + 1) * XK, :], xT[b, :, h * XK:(h + 1) * XK, :]
                             ).then_inc(x_raw_in[h], 16)

            def load_up(c):
                if c >= RING:
                    sp.wait_ge(up_ready, c - RING + 1)
                sp.dma_start(up_raw[:, c % RING, :], w_up[c, :, :]).then_inc(up_raw_in[c % RING], 16)

            def load_rows(b, t):
                if not (isinstance(b, int) and b == 0):
                    sp.wait_ge(stored[t], b * 16)
                sp.dma_start(rows[:, t, :], x[b, t * P:(t + 1) * P, :]).then_inc(rows_in[t], 16)

            def store_rows(b, t):
                sp.wait_ge(out_ready, (b * T + t + 1) * 2)
                sp.dma_start(out[b, t * P:(t + 1) * P, :], rows[:, t, :]).then_inc(stored[t], 16)

            load_x(0, 0)
            i = adapter(0)
            load_w(0, 0, i)
            load_x(0, 1)
            for c in range(1, RING):
                load_w(0, c, i)
            sp.dma_start(gl_raw[:, :, :], gl[:, :, :]).then_inc(gl_in, 16)
            for c in range(RING):
                load_up(c)
                load_w(0, RING + c, i)
            for k in range(4):
                sp.dma_start(lb_raw[k * ER:(k + 1) * ER, :], lora_b[:, :]).then_inc(lb_in, 16)
            sp.dma_start(bias_sb[:, :], bias[:, :]).then_inc(bias_in, 16)
            for h in range(XH):
                load_x(1, h)
            i = adapter(1)
            for c in range(RING):
                load_up(RING + c)
            for c in range(RING):
                load_w(1, c, i)
            for t in range(T):
                load_rows(0, t)
            with sp.Fori(0, B - 2) as b:
                i = adapter(b + 1)
                for c in range(RING, OC):
                    load_w(b + 1, c, i)
                for h in range(XH):
                    load_x(b + 2, h)
                for t in range(T):
                    store_rows(b, t)
                i = adapter(b + 2)
                for c in range(RING):
                    load_w(b + 2, c, i)
                for t in range(T):
                    load_rows(b + 1, t)
            i = adapter(B - 1)
            for c in range(RING, OC):
                load_w(B - 1, c, i)
            for t in range(T):
                store_rows(B - 2, t)
            for t in range(T):
                load_rows(B - 1, t)
            for t in range(T):
                store_rows(B - 1, t)
            for t in range(T):
                sp.wait_ge(stored[t], B * 16)

        @block.gpsimd
        def _(pool):
            pool.memset(eye_f[:, :], 0.0).then_inc(eye_step, 1)
            pool.wait_ge(eye_step, 1)
            pool.affine_select(out=eye_f[:, :], in_=eye_f[:, :], compare_op=ALU.not_equal, fill=1.0,
                               base=0, pattern=[[-1, P]], channel_multiplier=1).then_inc(eye_step, 1)
            for e in range(E):
                pool.memset(rank[:, e:e + 1], float(E - e)).then_inc(rank_ready, 1)

        @block.scalar
        def _(act):
            def x_hi(b, h):
                if not (isinstance(b, int) and b == 0):
                    act.wait_ge(y_done, b * OC)
                act.wait_ge(x_raw_in[h], (b + 1) * 16)
                act.copy(x_hilo[:, h * XK:(h + 1) * XK, 0:S], x_raw[:, h * XK:(h + 1) * XK, :]
                         ).then_inc(x_hi_ready, 1)

            def w_hi_part(b, c):
                if not (isinstance(b, int) and b == 0 and c < RING):
                    act.wait_ge(y_done, b * OC + c - RING + 1)
                act.wait_ge(w_raw_in[c % RING], (b * (OC // RING) + c // RING + 1) * 16)
                act.copy(w_hi[:, c % RING, :], w_raw[:, c % RING, :]).then_inc(w_hi_ready, 1)

            def up_hi_part(c):
                act.wait_ge(up_raw_in[c % RING], (c // RING + 1) * 16)
                act.copy(up_hi[:, c, 0:H], up_raw[:, c % RING, :]).then_inc(up_hi_ready, 1)

            def constants():
                act.wait_ge(gl_in, 16)
                act.copy(up_hi[:, :, H:H + GL], gl_raw[:, :, :]).then_inc(gl_hi_ready, 1)
                act.wait_ge(lb_in, 4 * 16)
                act.copy(lb_parts[:, :], lb_raw[:, :]).then_inc(lb_hi_ready, 1)
                act.wait_ge(eye_step, 2)
                act.copy(eye[:, :], eye_f[:, :]).then_inc(eye_ready, 1)

            def batch(b, first=False, last=False):
                for c in range(OC):
                    act.wait_ge(y_done, b * OC + c + 1)
                    act.copy(y_small[:, c % 2, :], ps_y[c % 2][:, S:2 * S]).then_inc(y_small_ready, 1)
                    if c < OC - RING:
                        w_hi_part(b, RING + c)
                    if first:
                        if c == RING - 1:
                            constants()
                        up_hi_part(c)
                    act.wait_ge(y_full_ready, b * OC + c + 1)
                    act.copy(y_hi[:, c, :], y_full[:, c % 2, :]).then_inc(y_hi_ready, 1)
                if not last:
                    for h in range(XH):
                        x_hi(b + 1, h)
                    for c in range(RING):
                        w_hi_part(b + 1, c)
                for t in range(T):
                    act.wait_ge(zt_done, b * T + t + 1)
                    act.copy(zT[:, t, :], ps_y[t][:, 0:P]).then_inc(zt_ready, 1)

            x_hi(0, 0)
            w_hi_part(0, 0)
            x_hi(0, 1)
            for c in range(1, RING):
                w_hi_part(0, c)
            batch(0, first=True)
            with act.Fori(1, B - 1) as b:
                batch(b)
            batch(B - 1, last=True)

        @block.vector
        def _(dve):
            def x_lo(b, h):
                dve.wait_ge(x_hi_ready, b * XH + h + 1)
                part = x_hilo[:, h * XK:(h + 1) * XK, :]
                dve.tensor_tensor(part[:, :, S:2 * S], x_raw[:, h * XK:(h + 1) * XK, :],
                                  part[:, :, 0:S].bitcast(F32), ALU.subtract).then_inc(x_ready, 1)

            def w_lo_part(b, c):
                dve.wait_ge(w_hi_ready, b * OC + c + 1)
                dve.tensor_tensor(w_lo[:, c % RING, :], w_raw[:, c % RING, :],
                                  w_hi[:, c % RING, :].bitcast(F32), ALU.subtract).then_inc(w_ready, 1)

            def up_lo_part(c):
                dve.wait_ge(up_hi_ready, c + 1)
                dve.tensor_tensor(up_lo[:, c, :], up_raw[:, c % RING, :],
                                  up_hi[:, c, 0:H].bitcast(F32), ALU.subtract).then_inc(up_ready, 1)

            def constants():
                dve.wait_ge(gl_hi_ready, 1)
                dve.tensor_tensor(up_hi[:, :, H + GL:NW], gl_raw[:, :, :],
                                  up_hi[:, :, H:H + GL].bitcast(F32), ALU.subtract).then_inc(gl_ready, 1)
                dve.wait_ge(lb_hi_ready, 1)
                for k in (1, 3):
                    part = slice(k * ER, (k + 1) * ER)
                    dve.tensor_tensor(lb_parts[part, :], lb_raw[part, :], lb_parts[part, :].bitcast(F32),
                                      ALU.subtract).then_inc(lb_ready, 1)

            def choose(b, t):
                n = b * T + t

                def link(i, ins):
                    ins.then_inc(z_step, 1)
                    dve.wait_ge(z_step, n * STEPS + i)

                ps = ps_o[t][:, 2, :]
                dve.wait_ge(z_done, n + 1)
                link(1, dve.tensor_copy(zlo[:, t, :], ps[:, BANK_C + GL:BANK_C + 2 * GL]))
                link(2, dve.tensor_tensor(zg[:, t, :], ps[:, BANK_C:BANK_C + GL], zlo[:, t, :], ALU.add))
                link(3, dve.tensor_tensor(lg[:, t, :], zg[:, t, ER:], bias_sb[:, :], ALU.add))
                link(4, dve.reduce_max(lmax[:, t:t + 1], lg[:, t, :], AX_X))
                link(5, dve.scalar_tensor_tensor(score[:, t, :], lg[:, t, :], lmax[:, t:t + 1], rank[:, :],
                                                 ALU.is_ge, ALU.mult))
                link(6, dve.reduce_max(smax[:, t:t + 1], score[:, t, :], AX_X))
                link(7, dve.scalar_tensor_tensor(
                    zm[:, t, :].rearrange("p (e r) -> p e r", r=R),
                    score[:, t, :].unsqueeze(2).to_broadcast([P, E, R]), smax[:, t:t + 1],
                    zg[:, t, 0:ER].rearrange("p (e r) -> p e r", r=R), ALU.is_equal, ALU.mult))
                twice = zm[:, t, :].unsqueeze(1).to_broadcast([P, 2, ER])
                hi = z_parts[:, t, 0:2 * ER].rearrange("p (k n) -> p k n", k=2)
                lo = z_parts[:, t, 2 * ER:].rearrange("p (k n) -> p k n", k=2)
                link(8, dve.tensor_copy(hi, twice))
                dve.tensor_tensor(lo, twice, hi.bitcast(F32), ALU.subtract).then_inc(z_parts_ready, 1)

            def finish(b, t):
                dve.wait_ge(out_done, b * T + t + 1)
                dve.wait_ge(rows_in[t], (b + 1) * 16)
                ab = rows[:, t, 0:2 * CUT].rearrange("p (k n) -> p k n", k=2)
                dve.tensor_tensor(ab, ps_o[t][:, 0:2, 0:CUT], ab, ALU.add).then_inc(out_ready, 1)
                dve.tensor_tensor(rows[:, t, 2 * CUT:], ps_o[t][:, 2, 0:BANK_C], rows[:, t, 2 * CUT:],
                                  ALU.add).then_inc(out_ready, 1)

            def batch(b, first=False, last=False):
                for c in range(OC):
                    dve.wait_ge(y_small_ready, b * OC + c + 1)
                    if c >= 2 or not first:
                        dve.wait_ge(y_hi_ready, b * OC + c - 1)
                    dve.tensor_tensor(y_full[:, c % 2, :], ps_y[c % 2][:, 0:S], y_small[:, c % 2, :],
                                      ALU.add).then_inc(y_full_ready, 1)
                    if c < OC - RING:
                        w_lo_part(b, RING + c)
                    if first:
                        if c == RING - 1:
                            constants()
                        up_lo_part(c)
                    dve.wait_ge(y_hi_ready, b * OC + c + 1)
                    dve.tensor_tensor(y_lo[:, c, :], y_full[:, c % 2, :], y_hi[:, c, :].bitcast(F32),
                                      ALU.subtract).then_inc(y_ready, 1)
                if not last:
                    for h in range(XH):
                        x_lo(b + 1, h)
                    for c in range(RING):
                        w_lo_part(b + 1, c)
                for t in range(T):
                    choose(b, t)
                for t in range(T):
                    finish(b, t)

            x_lo(0, 0)
            w_lo_part(0, 0)
            x_lo(0, 1)
            for c in range(1, RING):
                w_lo_part(0, c)
            dve.wait_ge(bias_in, 16)
            dve.wait_ge(rank_ready, E)
            batch(0, first=True)
            with dve.Fori(1, B - 1) as b:
                batch(b)
            batch(B - 1, last=True)

        @block.tensor
        def _(pe):
            def first_product(b):
                for c in range(OC):
                    pe.wait_ge(w_ready, b * OC + c + 1)
                    if c >= 2:
                        pe.wait_ge(y_full_ready, b * OC + c - 1)
                    for k in range(KC):
                        if c == 0 and k % XK == 0:
                            pe.wait_ge(x_ready, b * XH + k // XK + 1)
                        cols = slice(k * P, (k + 1) * P)
                        pe.matmul(ps_y[c % 2][:, :], w_hi[:, c % RING, cols], x_hilo[:, k, :],
                                  start=(k == 0), stop=False)
                        last = pe.matmul(ps_y[c % 2][:, S:2 * S], w_lo[:, c % RING, cols], x_hilo[:, k, 0:S],
                                         start=False, stop=(k == KC - 1))
                    last.then_inc(y_done, 1)

            def bank_ab(t, c):
                toks = slice(t * P, (t + 1) * P)
                for y, up in ((y_hi, up_hi), (y_hi, up_lo), (y_lo, up_hi)):
                    for k in range(2):
                        pe.matmul(ps_o[t][:, k, 0:CUT], y[:, c, toks], up[:, c, k * CUT:(k + 1) * CUT],
                                  start=(c == 0 and y is y_hi and up is up_hi), stop=False)

            def bank_c(t, c):
                toks = slice(t * P, (t + 1) * P)
                terms = [(y_hi, up_hi, NW), (y_hi, up_lo, H), (y_lo, up_hi, H + GL)]
                for y, up, end in terms if c < OC - 1 else terms[::-1]:
                    last = pe.matmul(ps_o[t][:, 2, 0:end - 2 * CUT], y[:, c, toks], up[:, c, 2 * CUT:end],
                                     start=(c == 0 and end == NW), stop=(c == OC - 1 and end == NW))
                if c == OC - 1:
                    last.then_inc(z_done, 1)

            def transpose_z(b, t):
                pe.wait_ge(z_parts_ready, b * T + t + 1)
                pe.matmul(ps_y[t][:, 0:P], z_parts[:, t, :], eye[:, :], start=True, stop=True
                          ).then_inc(zt_done, 1)

            def add_lora(b, t):
                pe.wait_ge(zt_ready, b * T + t + 1)
                for k, n in enumerate((CUT, CUT, BANK_C)):
                    last = pe.matmul(ps_o[t][:, k, 0:n], zT[:, t, :], lb_parts[:, k * CUT:k * CUT + n],
                                     start=False, stop=True, skip_group_check=(k == 2))
                last.then_inc(out_done, 1)

            with pe.Fori(0, B) as b:
                first_product(b)
                pe.wait_ge(gl_ready, 1)
                for c in range(OC):
                    pe.wait_ge(up_ready, c + 1)
                    pe.wait_ge(y_ready, b * OC + c + 1)
                    bank_ab(0, c)
                    bank_c(0, c)
                for c in range(OC):
                    bank_c(1, c)
                pe.wait_ge(eye_ready, 1)
                transpose_z(b, 0)
                for c in range(OC):
                    if c == OC - 1:
                        transpose_z(b, 1)
                    bank_ab(1, c)
                pe.wait_ge(lb_ready, 2)
                for t in range(T):
                    add_lora(b, t)


def kernel(x, itok_B_3_7, L0_cond_weight, L0_ffn_W_up, L0_ffn_gate_w, L0_ffn_expert_bias, L0_ffn_lora_A,
           L0_ffn_lora_B):
    import numpy as np
    import concourse.bacc as bacc
    from concourse.bass_utils import run_bass_kernel_spmd

    x, ids, w, w_up, gate_w, bias, lora_a, lora_b = (np.asarray(a) for a in (
        x, itok_B_3_7, L0_cond_weight, L0_ffn_W_up, L0_ffn_gate_w, L0_ffn_expert_bias, L0_ffn_lora_A,
        L0_ffn_lora_B))
    B, S, H = x.shape
    A = w.shape[0]
    E, R, _ = lora_a.shape
    C = H // P
    arrays = {
        "xT": x.reshape(B, S, C, P).transpose(0, 3, 2, 1),
        "x": x,
        "ids": ids.reshape(1, B),
        "w": w.reshape(A, C, P, C, P).transpose(0, 1, 4, 3, 2).reshape(A * C, P, H),
        "w_up": w_up.T.reshape(C, P, H),
        "gl": np.concatenate([lora_a.reshape(E * R, H), gate_w]).T.reshape(C, P, E * R + E).transpose(1, 0, 2),
        "lora_b": lora_b.transpose(0, 2, 1).reshape(E * R, H),
        "bias": np.broadcast_to(bias, (P, E)),
    }
    arrays = {k: np.ascontiguousarray(a) for k, a in arrays.items()}
    nc = bacc.Bacc("TRN2", target_bir_lowering=False, num_devices=1)
    args = {k: nc.dram_tensor(f"{k}_dram", a.shape, mybir.dt.from_np(a.dtype), kind="ExternalInput").ap()
            for k, a in arrays.items()}
    out = nc.dram_tensor("out_dram", x.shape, F32, kind="ExternalOutput").ap()
    build(nc, *args.values(), out)
    r = run_bass_kernel_spmd(nc, [{f"{k}_dram": a for k, a in arrays.items()}], core_ids=[0])
    return r.results[0]["out_dram"]
```

```python
from contextlib import ExitStack

import concourse.bass as bass
from concourse import mybir

P = 128
F32 = mybir.dt.float32
F32R = mybir.dt.float32r
I32 = mybir.dt.int32
ALU = mybir.AluOpType
AX_X = mybir.AxisListType.X


def build(nc, xT, x, ids, w, w_up, gl, lora_b, bias, out):
    B, S, H = x.shape
    KC = H // P
    OC = H // P
    T = S // P
    A = w.shape[0] // OC
    E = bias.shape[1]
    ER = lora_b.shape[0]
    R = ER // E
    GL = ER + E
    NW = H + 2 * GL
    RING = 4
    HALVES = 2
    HK = KC // HALVES
    XQ = 4
    XK = KC // XQ
    LAST = (2, 1, 0)
    UP_AFTER = {4: (0, 1), 5: (2, 3), 6: (4, 5), 7: (6, 7)}
    CUT = (NW // 3 + 1) // 2 * 2
    BANK_C = H - 2 * CUT
    STEPS = 8
    assert T == 2 and 4 * ER == P and BANK_C + 2 * GL <= 512 and B >= 3

    with ExitStack() as ctx:
        def sb(name, shape, dt=F32):
            return ctx.enter_context(nc.sbuf_tensor(name, shape, dt))

        def sem(name):
            return ctx.enter_context(nc.semaphore(name))

        w_raw = sb("w_raw", [P, RING, KC * P])
        w_hi = sb("w_hi", [P, RING, KC * P], F32R)
        w_lo = sb("w_lo", [P, RING, KC * P], F32R)
        x_raw = sb("x_raw", [P, KC, S])
        x_hilo = sb("x_hilo", [P, KC, 2 * S], F32R)
        up_raw = sb("up_raw", [P, RING, H])
        up_hi = sb("up_hi", [P, OC, NW], F32R)
        up_lo = sb("up_lo", [P, OC, H], F32R)
        gl_raw = sb("gl_raw", [P, OC, GL])
        y_small = sb("y_small", [P, 2, S])
        y_full = sb("y_full", [P, 2, S])
        y_hi = sb("y_hi", [P, OC, S], F32R)
        y_lo = sb("y_lo", [P, OC, S], F32R)
        rows = sb("rows", [P, T, H])
        lb_raw = sb("lb_raw", [P, H])
        lb_parts = sb("lb_parts", [P, H], F32R)
        bias_sb = sb("bias_sb", [P, E])
        rank = sb("rank", [P, E])
        eye_f = sb("eye_f", [P, P])
        eye = sb("eye", [P, P], F32R)
        zlo = sb("zlo", [P, T, GL])
        zg = sb("zg", [P, T, GL])
        lg = sb("lg", [P, T, E])
        lmax = sb("lmax", [P, T])
        score = sb("score", [P, T, E])
        smax = sb("smax", [P, T])
        zm = sb("zm", [P, T, ER])
        z_parts = sb("z_parts", [P, T, P], F32R)
        zT = sb("zT", [P, T, P], F32R)

        ps_y = [ctx.enter_context(nc.psum_tensor(f"ps_y{i}", [P, 512], F32)) for i in range(2)]
        ps_o = [ctx.enter_context(nc.psum_tensor(f"ps_o{t}", [P, 3, 512], F32)) for t in range(T)]

        x_raw_in = [sem(f"x_raw_in{q}") for q in range(XQ)]
        w_first_in = sem("w_first_in")
        w_raw_in = [sem(f"w_raw_in{s}") for s in range(RING)]
        up_raw_in = [sem(f"up_raw_in{s}") for s in range(RING)]
        rows_in = [sem(f"rows_in{t}") for t in range(T)]
        gl_in = sem("gl_in")
        lb_in = sem("lb_in")
        bias_in = sem("bias_in")
        x_hi_ready = sem("x_hi_ready")
        x_ready = sem("x_ready")
        w_hi_ready = sem("w_hi_ready")
        w_ready = sem("w_ready")
        up_hi_ready = sem("up_hi_ready")
        up_ready = [sem("up_ready_dve"), sem("up_ready_pool")]
        gl_hi_ready = sem("gl_hi_ready")
        gl_ready = sem("gl_ready")
        lb_hi_ready = sem("lb_hi_ready")
        lb_ready = sem("lb_ready")
        eye_step = sem("eye_step")
        eye_ready = sem("eye_ready")
        rank_ready = sem("rank_ready")
        y_done = sem("y_done")
        y_small_ready = sem("y_small_ready")
        y_full_ready = sem("y_full_ready")
        y_hi_ready = sem("y_hi_ready")
        y_ready = sem("y_ready")
        z_done = sem("z_done")
        z_step = sem("z_step")
        z_parts_ready = sem("z_parts_ready")
        zt_done = sem("zt_done")
        zt_ready = sem("zt_ready")
        out_done = sem("out_done")
        out_ready = sem("out_ready")
        stored = [sem(f"stored{t}") for t in range(T)]

        block = ctx.enter_context(nc.Block())

        @block.sync
        def _(sp):
            def adapter(b):
                i = sp.value_load(ids[0:1, b:b + 1] if isinstance(b, int) else ids[0:1, bass.ds(b, 1)])
                i = i + (i < 0) * A
                i = i * (i > -1)
                i = i + (i > A - 1) * (A - 1 - i)
                return sp.snap(i, min_val=0, max_val=A - 1)

            def load_w(b, c, i):
                if not (isinstance(b, int) and b == 0 and c < RING):
                    sp.wait_ge(w_ready, (b * OC + c - RING + 1) * HALVES)
                sp.dma_start(w_raw[:, c % RING, :], w[bass.ds(i * OC + c, 1), :, :].rearrange("a p n -> (a p) n")
                             ).then_inc(w_raw_in[c % RING], 16)

            def load_first_w(i, h):
                part = slice(h * HK * P, (h + 1) * HK * P)
                sp.dma_start(w_raw[:, 0, part], w[bass.ds(i * OC, 1), :, part].rearrange("a p n -> (a p) n")
                             ).then_inc(w_first_in if h == 0 else w_raw_in[0], 16)

            def load_x(b, q):
                if not (isinstance(b, int) and b == 0):
                    sp.wait_ge(x_ready, (b - 1) * XQ + q + 1)
                sp.dma_start(x_raw[:, q * XK:(q + 1) * XK, :], xT[b, :, q * XK:(q + 1) * XK, :]
                             ).then_inc(x_raw_in[q], 16)

            def load_up(c):
                if c >= RING:
                    sp.wait_ge(up_ready[c % 2], (c - RING) // 2 + 1)
                sp.dma_start(up_raw[:, c % RING, :], w_up[c, :, :]).then_inc(up_raw_in[c % RING], 16)

            def load_rows(b, t):
                if not (isinstance(b, int) and b == 0):
                    sp.wait_ge(stored[t], b * 16 * (t + 1))
                sp.dma_start(rows[:, t, :], x[b, t * P:(t + 1) * P, :]).then_inc(rows_in[t], 16)

            def store_rows(b, t):
                toks = slice(t * P, (t + 1) * P)
                if t == 0:
                    sp.wait_ge(out_ready, b * 6 + 3)
                    sp.dma_start(out[b, toks, :], rows[:, t, :]).then_inc(stored[t], 16)
                else:
                    sp.wait_ge(out_ready, b * 6 + 5)
                    sp.dma_start(out[b, toks, CUT:], rows[:, t, CUT:]).then_inc(stored[t], 16)
                    sp.wait_ge(out_ready, b * 6 + 6)
                    sp.dma_start(out[b, toks, 0:CUT], rows[:, t, 0:CUT]).then_inc(stored[t], 16)

            i = adapter(0)
            for h in range(HALVES):
                load_first_w(i, h)
            for q in range(XQ // 2, XQ):
                load_x(0, q)
            for c in range(1, OC):
                load_w(0, c, i)
            sp.dma_start(gl_raw[:, :, :], gl[:, :, :]).then_inc(gl_in, 16)
            for c in range(RING):
                load_up(c)
            for q in range(XQ):
                load_x(1, q)
            for c in range(RING, OC):
                load_up(c)
            for k in range(4):
                sp.dma_start(lb_raw[k * ER:(k + 1) * ER, :], lora_b[:, :]).then_inc(lb_in, 16)
            sp.dma_start(bias_sb[:, :], bias[:, :]).then_inc(bias_in, 16)
            i = adapter(1)
            for c in range(RING):
                load_w(1, c, i)
            for t in range(T):
                load_rows(0, t)
            with sp.Fori(0, B - 2) as b:
                i = adapter(b + 1)
                for c in range(RING, OC):
                    load_w(b + 1, c, i)
                for q in range(XQ):
                    load_x(b + 2, q)
                for t in range(T):
                    store_rows(b, t)
                i = adapter(b + 2)
                for c in range(RING):
                    load_w(b + 2, c, i)
                for t in range(T):
                    load_rows(b + 1, t)
            i = adapter(B - 1)
            for c in range(RING, OC):
                load_w(B - 1, c, i)
            for t in range(T):
                store_rows(B - 2, t)
            for t in range(T):
                load_rows(B - 1, t)
            for t in range(T):
                store_rows(B - 1, t)
            for t in range(T):
                sp.wait_ge(stored[t], B * 16 * (t + 1))

        @block.gpsimd
        def _(pool):
            pool.memset(eye_f[:, :], 0.0).then_inc(eye_step, 1)
            pool.wait_ge(eye_step, 1)
            pool.affine_select(out=eye_f[:, :], in_=eye_f[:, :], compare_op=ALU.not_equal, fill=1.0,
                               base=0, pattern=[[-1, P]], channel_multiplier=1).then_inc(eye_step, 1)
            for e in range(E):
                pool.memset(rank[:, e:e + 1], float(E - e)).then_inc(rank_ready, 1)
            pool.wait_ge(gl_hi_ready, 1)
            pool.tensor_tensor(up_hi[:, :, H + GL:NW], gl_raw[:, :, :], up_hi[:, :, H:H + GL].bitcast(F32),
                               ALU.subtract).then_inc(gl_ready, 1)
            for c in range(1, OC, 2):
                pool.wait_ge(up_hi_ready, c + 1)
                pool.tensor_tensor(up_lo[:, c, :], up_raw[:, c % RING, :], up_hi[:, c, 0:H].bitcast(F32),
                                   ALU.subtract).then_inc(up_ready[1], 1)
            pool.wait_ge(lb_hi_ready, 1)
            for i, k in enumerate((1, 3)):
                if i == 0:
                    pool.wait_ge(up_ready[1], OC // 2)
                else:
                    pool.wait_ge(lb_ready, 1)
                part = slice(k * ER, (k + 1) * ER)
                pool.tensor_tensor(lb_parts[part, :], lb_raw[part, :], lb_parts[part, :].bitcast(F32),
                                   ALU.subtract).then_inc(lb_ready, 1)

        @block.scalar
        def _(act):
            def x_hi(b, q):
                if not (isinstance(b, int) and b == 0):
                    act.wait_ge(y_done, b * OC)
                act.wait_ge(x_raw_in[q], (b + 1) * 16)
                act.copy(x_hilo[:, q * XK:(q + 1) * XK, 0:S], x_raw[:, q * XK:(q + 1) * XK, :]
                         ).then_inc(x_hi_ready, 1)

            def w_hi_part(b, c):
                if not (isinstance(b, int) and b == 0 and c < RING):
                    act.wait_ge(y_done, b * OC + c - RING + 1)
                for h in range(HALVES):
                    if isinstance(b, int) and (b, c, h) == (0, 0, 0):
                        act.wait_ge(w_first_in, 16)
                    else:
                        act.wait_ge(w_raw_in[c % RING], (b * (OC // RING) + c // RING + 1) * 16)
                    part = slice(h * HK * P, (h + 1) * HK * P)
                    act.copy(w_hi[:, c % RING, part], w_raw[:, c % RING, part]).then_inc(w_hi_ready, 1)

            def up_hi_part(c):
                act.wait_ge(up_raw_in[c % RING], (c // RING + 1) * 16)
                act.copy(up_hi[:, c, 0:H], up_raw[:, c % RING, :]).then_inc(up_hi_ready, 1)

            def gate_hi():
                act.wait_ge(gl_in, 16)
                act.copy(up_hi[:, :, H:H + GL], gl_raw[:, :, :]).then_inc(gl_hi_ready, 1)

            def lora_b_hi():
                act.wait_ge(lb_in, 4 * 16)
                act.copy(lb_parts[:, :], lb_raw[:, :]).then_inc(lb_hi_ready, 1)
                act.wait_ge(eye_step, 2)
                act.copy(eye[:, :], eye_f[:, :]).then_inc(eye_ready, 1)

            def batch(b, first=False, last=False):
                for c in range(OC):
                    act.wait_ge(y_done, b * OC + c + 1)
                    act.copy(y_small[:, c % 2, :], ps_y[c % 2][:, S:2 * S]).then_inc(y_small_ready, 1)
                    if c < OC - RING:
                        w_hi_part(b, RING + c)
                    act.wait_ge(y_full_ready, b * OC + c + 1)
                    act.copy(y_hi[:, c, :], y_full[:, c % 2, :]).then_inc(y_hi_ready, 1)
                    if first:
                        if c == min(UP_AFTER):
                            gate_hi()
                        for u in UP_AFTER.get(c, ()):
                            up_hi_part(u)
                if first:
                    lora_b_hi()
                if not last:
                    for q in range(XQ):
                        x_hi(b + 1, q)
                    for c in range(RING):
                        w_hi_part(b + 1, c)
                for t in range(T):
                    act.wait_ge(zt_done, b * T + t + 1)
                    act.copy(zT[:, t, :], ps_y[t][:, 0:P]).then_inc(zt_ready, 1)

            for q in range(XQ // 2):
                act.dma_start(x_raw[:, q * XK:(q + 1) * XK, :], xT[0, :, q * XK:(q + 1) * XK, :]
                              ).then_inc(x_raw_in[q], 16)
            for q in range(XQ // 2):
                x_hi(0, q)
            w_hi_part(0, 0)
            for q in range(XQ // 2, XQ):
                x_hi(0, q)
            for c in range(1, RING):
                w_hi_part(0, c)
            batch(0, first=True)
            with act.Fori(1, B - 1) as b:
                batch(b)
            batch(B - 1, last=True)

        @block.vector
        def _(dve):
            def x_lo(b, q):
                dve.wait_ge(x_hi_ready, b * XQ + q + 1)
                part = x_hilo[:, q * XK:(q + 1) * XK, :]
                dve.tensor_tensor(part[:, :, S:2 * S], x_raw[:, q * XK:(q + 1) * XK, :],
                                  part[:, :, 0:S].bitcast(F32), ALU.subtract).then_inc(x_ready, 1)

            def w_lo_part(b, c):
                for h in range(HALVES):
                    dve.wait_ge(w_hi_ready, (b * OC + c) * HALVES + h + 1)
                    part = slice(h * HK * P, (h + 1) * HK * P)
                    dve.tensor_tensor(w_lo[:, c % RING, part], w_raw[:, c % RING, part],
                                      w_hi[:, c % RING, part].bitcast(F32), ALU.subtract).then_inc(w_ready, 1)

            def up_lo_part(c):
                dve.wait_ge(up_hi_ready, c + 1)
                dve.tensor_tensor(up_lo[:, c, :], up_raw[:, c % RING, :],
                                  up_hi[:, c, 0:H].bitcast(F32), ALU.subtract).then_inc(up_ready[0], 1)

            def choose(b, t):
                n = b * T + t

                def link(i, ins):
                    ins.then_inc(z_step, 1)
                    dve.wait_ge(z_step, n * STEPS + i)

                ps = ps_o[t][:, 2, :]
                dve.wait_ge(z_done, n + 1)
                link(1, dve.tensor_copy(zlo[:, t, :], ps[:, BANK_C + GL:BANK_C + 2 * GL]))
                link(2, dve.tensor_tensor(zg[:, t, :], ps[:, BANK_C:BANK_C + GL], zlo[:, t, :], ALU.add))
                link(3, dve.tensor_tensor(lg[:, t, :], zg[:, t, ER:], bias_sb[:, :], ALU.add))
                link(4, dve.reduce_max(lmax[:, t:t + 1], lg[:, t, :], AX_X))
                link(5, dve.scalar_tensor_tensor(score[:, t, :], lg[:, t, :], lmax[:, t:t + 1], rank[:, :],
                                                 ALU.is_ge, ALU.mult))
                link(6, dve.reduce_max(smax[:, t:t + 1], score[:, t, :], AX_X))
                link(7, dve.scalar_tensor_tensor(
                    zm[:, t, :].rearrange("p (e r) -> p e r", r=R),
                    score[:, t, :].unsqueeze(2).to_broadcast([P, E, R]), smax[:, t:t + 1],
                    zg[:, t, 0:ER].rearrange("p (e r) -> p e r", r=R), ALU.is_equal, ALU.mult))
                twice = zm[:, t, :].unsqueeze(1).to_broadcast([P, 2, ER])
                hi = z_parts[:, t, 0:2 * ER].rearrange("p (k n) -> p k n", k=2)
                lo = z_parts[:, t, 2 * ER:].rearrange("p (k n) -> p k n", k=2)
                link(8, dve.tensor_copy(hi, twice))
                dve.tensor_tensor(lo, twice, hi.bitcast(F32), ALU.subtract).then_inc(z_parts_ready, 1)

            def finish(b, t):
                dve.wait_ge(rows_in[t], (b + 1) * 16)
                for i, k in enumerate(range(3) if t == 0 else LAST):
                    dve.wait_ge(out_done, (b * T + t) * 3 + i + 1)
                    part = slice(k * CUT, min((k + 1) * CUT, H))
                    dve.tensor_tensor(rows[:, t, part], ps_o[t][:, k, 0:part.stop - part.start],
                                      rows[:, t, part], ALU.add).then_inc(out_ready, 1)

            def batch(b, first=False, last=False):
                for c in range(OC):
                    dve.wait_ge(y_small_ready, b * OC + c + 1)
                    if c >= 2 or not first:
                        dve.wait_ge(y_hi_ready, b * OC + c - 1)
                    dve.tensor_tensor(y_full[:, c % 2, :], ps_y[c % 2][:, 0:S], y_small[:, c % 2, :],
                                      ALU.add).then_inc(y_full_ready, 1)
                    if c < OC - RING:
                        w_lo_part(b, RING + c)
                    dve.wait_ge(y_hi_ready, b * OC + c + 1)
                    dve.tensor_tensor(y_lo[:, c, :], y_full[:, c % 2, :], y_hi[:, c, :].bitcast(F32),
                                      ALU.subtract).then_inc(y_ready, 1)
                    if first:
                        for u in UP_AFTER.get(c, ()):
                            if u % 2 == 0:
                                up_lo_part(u)
                if not last:
                    for q in range(XQ):
                        x_lo(b + 1, q)
                    for c in range(RING // 2):
                        w_lo_part(b + 1, c)
                if first:
                    dve.wait_ge(bias_in, 16)
                    dve.wait_ge(rank_ready, E)
                for t in range(T):
                    choose(b, t)
                if not last:
                    for c in range(RING // 2, RING):
                        w_lo_part(b + 1, c)
                for t in range(T):
                    finish(b, t)

            for q in range(XQ // 2):
                x_lo(0, q)
            w_lo_part(0, 0)
            for q in range(XQ // 2, XQ):
                x_lo(0, q)
            for c in range(1, RING):
                w_lo_part(0, c)
            batch(0, first=True)
            with dve.Fori(1, B - 1) as b:
                batch(b)
            batch(B - 1, last=True)

        @block.tensor
        def _(pe):
            def first_product(b):
                for c in range(OC):
                    if c >= 2:
                        pe.wait_ge(y_full_ready, b * OC + c - 1)
                    for k in range(KC):
                        if k % HK == 0:
                            pe.wait_ge(w_ready, (b * OC + c) * HALVES + k // HK + 1)
                        if c == 0 and k % XK == 0:
                            pe.wait_ge(x_ready, b * XQ + k // XK + 1)
                        cols = slice(k * P, (k + 1) * P)
                        pe.matmul(ps_y[c % 2][:, :], w_hi[:, c % RING, cols], x_hilo[:, k, :],
                                  start=(k == 0), stop=False)
                        last = pe.matmul(ps_y[c % 2][:, S:2 * S], w_lo[:, c % RING, cols], x_hilo[:, k, 0:S],
                                         start=False, stop=(k == KC - 1))
                    last.then_inc(y_done, 1)

            def bank_ab(t, c, banks=(0, 1)):
                toks = slice(t * P, (t + 1) * P)
                for n, (y, up) in enumerate(((y_hi, up_hi), (y_hi, up_lo), (y_lo, up_hi))):
                    for k in banks:
                        pe.matmul(ps_o[t][:, k, 0:CUT], y[:, c, toks], up[:, c, k * CUT:(k + 1) * CUT],
                                  start=(c == 0 and n == 0), stop=False)

            def bank_c(t, c):
                toks = slice(t * P, (t + 1) * P)
                terms = [(y_hi, up_hi, NW), (y_hi, up_lo, H), (y_lo, up_hi, H + GL)]
                for y, up, end in terms if c < OC - 1 else terms[::-1]:
                    last = pe.matmul(ps_o[t][:, 2, 0:end - 2 * CUT], y[:, c, toks], up[:, c, 2 * CUT:end],
                                     start=(c == 0 and end == NW), stop=(c == OC - 1 and end == NW))
                if c == OC - 1:
                    last.then_inc(z_done, 1)

            def transpose_z(b, t):
                pe.wait_ge(z_parts_ready, b * T + t + 1)
                pe.matmul(ps_y[t][:, 0:P], z_parts[:, t, :], eye[:, :], start=True, stop=True
                          ).then_inc(zt_done, 1)

            def add_lora(t, k):
                part = slice(k * CUT, min((k + 1) * CUT, H))
                pe.matmul(ps_o[t][:, k, 0:part.stop - part.start], zT[:, t, :], lb_parts[:, part],
                          start=False, stop=True, skip_group_check=(k == 2)).then_inc(out_done, 1)

            with nc.Fori(0, B, engines=(mybir.EngineType.PE,), hint_back_edge=True) as b:
                first_product(b)
                pe.wait_ge(gl_ready, 1)
                for c in range(OC):
                    pe.wait_ge(up_ready[c % 2], c // 2 + 1)
                    pe.wait_ge(y_ready, b * OC + c + 1)
                    bank_ab(0, c)
                    bank_c(0, c)
                for c in range(OC):
                    bank_c(1, c)
                pe.wait_ge(eye_ready, 1)
                for c in range(OC):
                    if c == OC // 2:
                        transpose_z(b, 0)
                    if c == OC - 1:
                        transpose_z(b, 1)
                    bank_ab(1, c, (1,))
                pe.wait_ge(lb_ready, 2)
                pe.wait_ge(zt_ready, b * T + 1)
                for k in range(3):
                    add_lora(0, k)
                pe.wait_ge(zt_ready, b * T + 2)
                add_lora(1, 2)
                add_lora(1, 1)
                for c in range(OC):
                    bank_ab(1, c, (0,))
                add_lora(1, 0)


def kernel(x, itok_B_3_7, L0_cond_weight, L0_ffn_W_up, L0_ffn_gate_w, L0_ffn_expert_bias, L0_ffn_lora_A,
           L0_ffn_lora_B):
    import numpy as np
    import concourse.bacc as bacc
    from concourse.bass_utils import run_bass_kernel_spmd

    x, ids, w, w_up, gate_w, bias, lora_a, lora_b = (np.asarray(a) for a in (
        x, itok_B_3_7, L0_cond_weight, L0_ffn_W_up, L0_ffn_gate_w, L0_ffn_expert_bias, L0_ffn_lora_A,
        L0_ffn_lora_B))
    B, S, H = x.shape
    A = w.shape[0]
    E, R, _ = lora_a.shape
    C = H // P
    arrays = {
        "xT": x.reshape(B, S, C, P).transpose(0, 3, 2, 1),
        "x": x,
        "ids": ids.reshape(1, B),
        "w": w.reshape(A, C, P, C, P).transpose(0, 1, 4, 3, 2).reshape(A * C, P, H),
        "w_up": w_up.T.reshape(C, P, H),
        "gl": np.concatenate([lora_a.reshape(E * R, H), gate_w]).T.reshape(C, P, E * R + E).transpose(1, 0, 2),
        "lora_b": lora_b.transpose(0, 2, 1).reshape(E * R, H),
        "bias": np.broadcast_to(bias, (P, E)),
    }
    arrays = {k: np.ascontiguousarray(a) for k, a in arrays.items()}
    nc = bacc.Bacc("TRN2", target_bir_lowering=False, num_devices=1)
    args = {k: nc.dram_tensor(f"{k}_dram", a.shape, mybir.dt.from_np(a.dtype), kind="ExternalInput").ap()
            for k, a in arrays.items()}
    out = nc.dram_tensor("out_dram", x.shape, F32, kind="ExternalOutput").ap()
    build(nc, *args.values(), out)
    r = run_bass_kernel_spmd(nc, [{f"{k}_dram": a for k, a in arrays.items()}], core_ids=[0])
    return r.results[0]["out_dram"]
```
